# Optimizing a Trainium2 kernel written in Bass

```python
import numpy as np
import jax
import jax.numpy as jnp

def _softmax(x, axis=-1):
    return jax.nn.softmax(x, axis=axis)

def _gelu(x):
    return jax.nn.gelu(x, approximate=True)

def _silu(x):
    return jax.nn.silu(x)

def _sigmoid(x):
    return jax.nn.sigmoid(x)

def _layernorm(x, axis=-1, eps=1e-05):
    m = jnp.mean(x, axis=axis, keepdims=True)
    v = jnp.var(x, axis=axis, keepdims=True)
    return (x - m) / jnp.sqrt(v + eps)

def _scatter_add(tgt, idx, src, axis=0):
    return tgt.at[idx].add(src)

def _segment_sum(src, seg, n):
    return jax.ops.segment_sum(src, seg, n)
kernel_name = 'mk_adaln_ffn_d1_seqx_r4_b4e9ee'

def setup_inputs(seed: int=0):
    np.random.seed(seed)
    _w = jnp.asarray

    def _rec_inputs():
        import jax
        import jax.numpy as jnp
        _rk = jax.random.key(seed)
        x = -8.015e-05 + 0.9999 * jax.random.normal(jax.random.fold_in(_rk, 1), (32, 64, 512), jnp.float32)
        _lenS = 64 - jax.random.randint(jax.random.fold_in(_rk, 7), (32,), 0, max(1, 64 // 4) + 1, jnp.int32)
        _lenS2 = 64 - jax.random.randint(jax.random.fold_in(_rk, 8), (32,), 0, max(1, 64 // 4) + 1, jnp.int32)
        cond_1024 = 0.00191187 + 0.999416 * jax.random.normal(jax.random.fold_in(_rk, 11), (32, 256), jnp.float32)
        return (x, cond_1024)
    x, cond_1024 = _rec_inputs()

    def _L0_cond_setup():
        import jax, jax.numpy as jnp
        import numpy as np
        B, N, V_DIM, Q_DIM = (64, 100, 512, 256)
        key = jax.random.key(seed)
        k1, k2, k3, k4 = jax.random.split(key, 4)
        v = jax.random.normal(k1, (B, N, V_DIM), dtype=jnp.float32)
        q = jax.random.normal(k2, (B, Q_DIM), dtype=jnp.float32)
        W3 = jax.random.normal(k3, (Q_DIM, V_DIM), dtype=jnp.float32) * (1.0 / np.sqrt(Q_DIM))
        b3 = jnp.zeros((V_DIM,), dtype=jnp.float32)
        W2 = jax.random.normal(k4, (V_DIM, V_DIM), dtype=jnp.float32) * (1.0 / np.sqrt(V_DIM))
        b2 = jnp.zeros((V_DIM,), dtype=jnp.float32)
        return {'v': v, 'q': q, 'W3': W3, 'b3': b3, 'W2': W2, 'b2': b2}
    _L0_cond_all = _L0_cond_setup()
    _L0_cond_in = {k: v for k, v in _L0_cond_all.items() if k in ('W3', 'b3', 'W2', 'b2')}
    del _L0_cond_all

    def _L0_ffn_setup():
        import jax, jax.numpy as jnp
        import numpy as np
        DIM = 512
        HIDDEN = 2048
        GROUP = 64

        def _ternary_weight(w, group_size):
            wb = w.astype(jnp.bfloat16)
            wg = wb.reshape(-1, group_size)
            scale = jnp.clip(jnp.mean(jnp.abs(wg), axis=-1, keepdims=True), 1e-08, None)
            q = jnp.clip(jnp.round(wg / scale), -1.0, 1.0)
            qs = (q * scale).reshape(w.shape).astype(w.dtype)
            return w + jax.lax.stop_gradient(qs - w)

        def _rms_norm(x):
            eps = jnp.asarray(jnp.finfo(x.dtype).eps, x.dtype)
            ms = jnp.mean(jnp.square(x), axis=-1, keepdims=True)
            return x * jax.lax.rsqrt(ms + eps)
        key = jax.random.key(seed)
        k_x, k_fc, k_proj = jax.random.split(key, 3)
        x = jax.random.normal(k_x, (4, 1024, DIM), dtype=jnp.float32)
        W_fc = jax.random.normal(k_fc, (HIDDEN, DIM), dtype=jnp.float32) / np.sqrt(DIM)
        W_proj = jax.random.normal(k_proj, (DIM, HIDDEN), dtype=jnp.float32) / np.sqrt(HIDDEN)
        return {'x': x, 'W_fc': W_fc, 'W_proj': W_proj}
    _L0_ffn_all = _L0_ffn_setup()
    _L0_ffn_in = {k: v for k, v in _L0_ffn_all.items() if k in ('W_fc', 'W_proj')}
    del _L0_ffn_all
    return {'x': x, 'cond_1024': cond_1024, 'L0_cond_W3': _L0_cond_in['W3'], 'L0_cond_b3': _L0_cond_in['b3'], 'L0_cond_W2': _L0_cond_in['W2'], 'L0_cond_b2': _L0_cond_in['b2'], 'L0_ffn_W_fc': _L0_ffn_in['W_fc'], 'L0_ffn_W_proj': _L0_ffn_in['W_proj']}

def reference(x, cond_1024, L0_cond_W3, L0_cond_b3, L0_cond_W2, L0_cond_b2, L0_ffn_W_fc, L0_ffn_W_proj):
    import jax
    import jax.numpy as jnp

    def _L0_cond_ref(v, q, W3, b3, W2, b2):
        import jax, jax.numpy as jnp
        import numpy as np
        B, N, V_DIM, Q_DIM = (64, 100, 512, 256)
        q_emb = jax.nn.relu(q @ W3 + b3)
        n = v.shape[1]
        v_sum = jnp.sum(v, axis=1, keepdims=True)
        x = (n * v + v_sum) * q_emb[:, None, :]
        return jax.nn.relu(x @ W2 + b2)

    def _L0_ffn_ref(x, W_fc, W_proj):
        import jax, jax.numpy as jnp
        import numpy as np
        DIM = 512
        HIDDEN = 2048
        GROUP = 64

        def _ternary_weight(w, group_size):
            wb = w.astype(jnp.bfloat16)
            wg = wb.reshape(-1, group_size)
            scale = jnp.clip(jnp.mean(jnp.abs(wg), axis=-1, keepdims=True), 1e-08, None)
            q = jnp.clip(jnp.round(wg / scale), -1.0, 1.0)
            qs = (q * scale).reshape(w.shape).astype(w.dtype)
            return w + jax.lax.stop_gradient(qs - w)

        def _rms_norm(x):
            eps = jnp.asarray(jnp.finfo(x.dtype).eps, x.dtype)
            ms = jnp.mean(jnp.square(x), axis=-1, keepdims=True)
            return x * jax.lax.rsqrt(ms + eps)
        w1 = _ternary_weight(W_fc, GROUP)
        h = jnp.einsum('bsd,hd->bsh', x, w1)
        h = jnp.square(jax.nn.relu(h))
        hn = _rms_norm(h)
        w2 = _ternary_weight(W_proj, GROUP)
        return jnp.einsum('bsh,dh->bsd', hn, w2)
    x = x + _L0_ffn_ref(_L0_cond_ref(x, cond_1024, L0_cond_W3, L0_cond_b3, L0_cond_W2, L0_cond_b2), L0_ffn_W_fc, L0_ffn_W_proj)
    return x

_drawn_inputs = setup_inputs


def setup_inputs(seed=0):
    import zlib

    import numpy as np

    out = dict(_drawn_inputs(seed))
    spreads = {'L0_cond_b3': (0.0, 0.1), 'L0_cond_b2': (0.0, 0.1)}
    factors = {}
    for name, (base, spread) in spreads.items():
        noise = np.random.default_rng([zlib.crc32(name.encode()), seed]).standard_normal(out[name].shape)
        drawn = base * np.exp(spread * noise) if base else spread * noise
        out[name] = jnp.asarray(drawn.astype(out[name].dtype))
    for name, factor in factors.items():
        out[name] = (out[name] * factor).astype(out[name].dtype)
    return out
```

```python
from contextlib import ExitStack

import concourse.bass as bass
from concourse import mybir

ALU = mybir.AluOpType
ACT = mybir.ActivationFunctionType
AX = mybir.AxisListType
F32 = mybir.dt.float32
F32R = mybir.dt.float32r
BF16 = mybir.dt.bfloat16

P = 128
BANK = 512
TERN_GROUP = 64
MIN_SCALE = 1e-8
RMS_EPS = 2.0 ** -23

RING = 2
SQ_RING = 4
RAW_RING = 4
WARM_UP = 12


def wait(engine, semaphore, count):
    if not isinstance(count, int) or count > 0:
        engine.wait_ge(semaphore, count)


def adaln_ffn(
    nc: bass.Bass,
    x: bass.AP,
    cond: bass.AP,
    w_q: bass.AP,
    b_q: bass.AP,
    w_v: bass.AP,
    b_v: bass.AP,
    w_fc: bass.AP,
    w_proj: bass.AP,
    out: bass.AP,
):
    BATCHES, N, D = x.shape
    Q = cond.shape[1]
    H = w_fc.shape[0]
    GROUPS = BATCHES * N // BANK
    TT = BANK // P
    KD = D // P
    KQ = Q // P
    HJ = H // P
    GB = BANK // N
    SG = 2 * BANK // TERN_GROUP
    assert D == BANK and GROUPS > 2 and TT == 4 and KD == 4

    def fc_pair(a):
        return w_fc[2 * a * P:2 * (a + 1) * P, :].rearrange("(i p) d -> p i d", p=P), 2 * a

    def proj_pair(c, a):
        return (w_proj[2 * a * P:2 * (a + 1) * P, c * BANK:(c + 1) * BANK].rearrange("(i p) h -> p i h", p=P),
                HJ + KD * c + 2 * a)

    PAIRS = []
    for c in range(HJ // TT):
        PAIRS += [fc_pair(2 * c), proj_pair(c, 0), proj_pair(c, 1), fc_pair(2 * c + 1)]
    EARLY = 4
    ON_PE = set(range(EARLY)) | {len(PAIRS) - 1}
    X_AT, H0_AT = {1: 1, 2: 2, 3: 3}, {4: 0, 6: 1, 8: 2, 10: 3}
    LATER_X_AT, LATER_H0_AT = {1: 0, 3: 1, 5: 2, 7: 3}, {9: 0, 10: 1, 12: 2, 13: 3}
    FINISH_AT = {2: 0, 4: 1, 6: 2, 8: 3}

    def beside(g):
        return (X_AT, H0_AT) if isinstance(g, int) and g == 0 else (LATER_X_AT, LATER_H0_AT)

    def sums_by_vector(g):
        return not isinstance(g, int) or g > 1

    x_rows = x.rearrange("b n d -> (b n) d").rearrange("(g t p) d -> g p t d", p=P, t=TT)
    out_rows = out.rearrange("b n d -> (b n) d").rearrange("(g t p) d -> g t p d", p=P, t=TT)

    with ExitStack() as ctx:
        def sb(name, shape, dt):
            return ctx.enter_context(nc.sbuf_tensor(name, shape, dt))

        def psum(name, shape, dt):
            return ctx.enter_context(nc.psum_tensor(name, shape, dt))

        def sem(name):
            return ctx.enter_context(nc.semaphore(name))

        sum_mat = sb("sum_mat", [P, P], F32)
        ident_b = sb("ident_b", [P, P], BF16)
        ident_f = sb("ident_f", [P, P], F32)
        ones = sb("ones", [P, 1], F32)
        cond_sb = sb("cond_sb", [BATCHES, Q], F32)
        cond_t = sb("cond_t", [P, KQ, BATCHES], F32)
        bq_t = sb("bq_t", [P, KD], F32)
        bv_t = sb("bv_t", [P, KD], F32)
        q_t = sb("q_t", [P, KD, BATCHES], F32)
        wv_sb = sb("wv_sb", [P, KD, D], F32)
        x_sb = sb("x_sb", [P, TT, D], F32)
        x_res = sb("x_res", [P, TT, D], F32)
        x1_t = sb("x1_t", [P, KD, BANK], F32)
        h0_f = sb("h0_f", [P, RING, BANK], F32)
        h0_hi = sb("h0_hi", [P, KD, RING * BANK], F32R)
        h0_lo = sb("h0_lo", [P, KD, RING * BANK], F32R)
        w_t = sb("w_t", [P, 2 * HJ, BANK], F32R)
        raw = sb("raw", [P, RAW_RING, 2 * BANK], F32)
        w_abs = sb("w_abs", [P, RING, 2 * BANK], BF16)
        w_sign = sb("w_sign", [P, RING, 2 * BANK], BF16)
        w_signed = sb("w_signed", [P, RING, 2 * BANK], BF16)
        w_mask = sb("w_mask", [P, RING, 2 * BANK], BF16)
        w_tern = sb("w_tern", [P, RING, 2 * BANK], BF16)
        w_turned = sb("w_turned", [P, 2 * TT, P], BF16)
        batch_sum = sb("batch_sum", [P, GB], F32)
        abs_sum = sb("abs_sum", [P, SG], F32)
        scale = sb("scale", [P, RING, SG], BF16)
        relu_y = sb("relu_y", [P, RING, BANK], F32)
        y = sb("y", [P, RING, BANK], F32)
        y_sq = sb("y_sq", [P, SQ_RING, BANK], F32)
        y_hi = sb("y_hi", [P, RING, BANK], F32R)
        y_lo = sb("y_lo", [P, RING, BANK], F32R)
        sq_acc = sb("sq_acc", [P, BANK], F32)
        mean_sq = sb("mean_sq", [P, TT], F32)
        root = sb("root", [P, TT], F32)
        rstd0 = sb("rstd0", [P, TT], F32)
        rsq = sb("rsq", [P, TT], F32)
        half = sb("half", [P, TT], F32)
        rstd = sb("rstd", [P, TT], F32)
        o_sb = sb("o_sb", [P, TT, D], F32)
        wq_sb = o_sb[:, 0:KQ, :]

        ps_out = psum("ps_out", [P, TT, BANK], F32)
        ps_acc = psum("ps_acc", [P, RING, BANK], F32)
        ps_x = psum("ps_x", [P, BANK], F32)
        ps_tr = psum("ps_tr", [P, 2 * BANK], BF16)
        ps_sq = ps_x[:, 0:TT]

        consts_ready = sem("consts_ready")
        cleared = sem("cleared")
        cond_loaded = sem("cond_loaded")
        wq_loaded = sem("wq_loaded")
        bias_loaded = sem("bias_loaded")
        wv_loaded = [sem(f"wv_loaded{i}") for i in range(2)]
        x0_loaded = [sem(f"x0_loaded{t}") for t in range(TT)]
        x_loaded = sem("x_loaded")
        res_loaded = sem("res_loaded")
        raw_loaded = [sem(f"raw_loaded{i}") for i in range(RAW_RING)]
        condt_done = sem("condt_done")
        condt_ready = sem("condt_ready")
        q_done = sem("q_done")
        q_ready = sem("q_ready")
        xt_done = sem("xt_done")
        summed = sem("summed")
        x1_ready = sem("x1_ready")
        h0_done = sem("h0_done")
        h0_relued = sem("h0_relued")
        h0_hi_done = sem("h0_hi_done")
        h0_split = sem("h0_split")
        abs_ready = sem("abs_ready")
        sign_ready = sem("sign_ready")
        sum_ready = sem("sum_ready")
        scale_ready = sem("scale_ready")
        masked = sem("masked")
        signed = sem("signed")
        tern_ready = sem("tern_ready")
        tr_done = sem("tr_done")
        turned = sem("turned")
        wt_ready = sem("wt_ready")
        hid_done = sem("hid_done")
        relued = sem("relued")
        y_ready = sem("y_ready")
        sq_ready = sem("sq_ready")
        sq_added = sem("sq_added")
        hi_done = sem("hi_done")
        split = sem("split")
        projected = sem("projected")
        tile_summed = sem("tile_summed")
        sq_summed = sem("sq_summed")
        mean_ready = sem("mean_ready")
        root_ready = sem("root_ready")
        newton = sem("newton")
        rstd_ready = sem("rstd_ready")
        even_copied = sem("even_copied")
        odd_copied = sem("odd_copied")
        finished = sem("finished")
        stored = sem("stored")

        block = ctx.enter_context(nc.Block())

        def turned_at(i):
            on_pe = sum(k in ON_PE for k in range(i + 1))
            return (tr_done, on_pe) if i in ON_PE else (turned, 16 * (i + 1 - on_pe))

        def rest_of_h0(engine, g, m):
            cols = bass.ds(g % RING * BANK, BANK)
            engine.wait_ge(h0_hi_done, KD * g + m + 1)
            engine.tensor_tensor(h0_lo[:, m, cols], h0_f[:, m % RING, :], h0_hi[:, m, cols], ALU.subtract).then_inc(h0_split, 1)

        def add_squares(engine, g, j):
            u = HJ * g + j
            engine.wait_ge(sq_ready, u + 1)
            if j == 1:
                wait(engine, sq_summed, g)
                engine.tensor_tensor(sq_acc[:], y_sq[:, 0, :], y_sq[:, 1, :], ALU.add).then_inc(sq_added, 2)
            else:
                engine.wait_ge(sq_added, u)
                engine.tensor_tensor(sq_acc[:], sq_acc[:], y_sq[:, j % SQ_RING, :], ALU.add).then_inc(sq_added, 1)

        @block.sync
        def _(sp):
            def load_pair(i):
                wait(sp, sign_ready, i - RAW_RING + 1)
                sp.dma_start(raw[:, i % RAW_RING, :].rearrange("p (i w) -> p i w", i=2), PAIRS[i][0]
                             ).then_inc(raw_loaded[i % RAW_RING], 16)

            def turn_pair(i):
                sp.wait_ge(tern_ready, i + 1)
                sp.wait_ge(wt_ready, i)
                sp.dma_start_transpose(out=w_turned[:], in_=w_tern[:, i % RING, :]).then_inc(turned, 16)

            def load_wv(i):
                cols = slice(i * D // 2, (i + 1) * D // 2)
                sp.dma_start(wv_sb[:, :, cols], w_v[:, cols].rearrange("(k p) d -> p k d", p=P)
                             ).then_inc(wv_loaded[i], 16)

            def load_x(dst, g, done):
                sp.dma_start(dst[:], x_rows[bass.ds(g, 1)].rearrange("g p t d -> p (g t) d")).then_inc(done, 16)

            sp.dma_start(cond_sb[:], cond).then_inc(cond_loaded, 16)
            for t in range(TT):
                if t == TT - 1:
                    sp.dma_start(wq_sb, w_q.rearrange("(k p) d -> p k d", p=P)).then_inc(wq_loaded, 16)
                sp.dma_start(x_sb[:, t, :], x_rows[0, :, t, :]).then_inc(x0_loaded[t], 16)
            load_wv(0)
            load_pair(0)
            load_pair(1)
            load_wv(1)
            for i in range(2, RAW_RING + 1):
                load_pair(i)
            sp.wait_ge(xt_done, KD)
            load_x(x_sb, 1, x_loaded)
            for i in range(RAW_RING + 1, EARLY + RAW_RING):
                load_pair(i)
            for i in range(EARLY, len(PAIRS)):
                if i + RAW_RING < len(PAIRS):
                    load_pair(i + RAW_RING)
                if i not in ON_PE:
                    turn_pair(i)

            def store(g):
                for t in range(TT):
                    sp.wait_ge(finished, TT * g + t + 1)
                    sp.dma_start(out_rows[bass.ds(g, 1), t].rearrange("g p d -> p (g d)"), o_sb[:, t, :]
                                 ).then_inc(stored, 16)

            load_x(x_res, 0, res_loaded)
            sp.wait_ge(xt_done, KD * 2)
            load_x(x_sb, 2, x_loaded)
            with sp.Fori(1, GROUPS - 2) as g:
                store(g - 1)
                load_x(x_res, g, res_loaded)
                sp.wait_ge(xt_done, KD * (g + 2))
                load_x(x_sb, g + 2, x_loaded)
            for g in range(GROUPS - 2, GROUPS):
                store(g - 1)
                load_x(x_res, g, res_loaded)
            store(GROUPS - 1)
            sp.wait_ge(stored, 16 * TT * GROUPS)

        @block.tensor
        def _(pe):
            def sum_x_block(t, k, dst):
                return pe.matmul(dst[:, t * P:(t + 1) * P], x_sb[:, t, k * P:(k + 1) * P], sum_mat[:], start=True, stop=True)

            def transpose_x(g, k):
                if k == 0:
                    pe.wait_ge(x_loaded, 16 * g)
                for t in range(TT):
                    if sums_by_vector(g):
                        last = pe.transpose(ps_x[:, t * P:(t + 1) * P], x_sb[:, t, k * P:(k + 1) * P], ident_f[:])
                    else:
                        last = sum_x_block(t, k, ps_x)
                last.then_inc(xt_done, 1)

            def make_h0(g, m, dst):
                pe.wait_ge(wv_loaded[m // 2], 16)
                for k in range(KD):
                    if m == 0:
                        pe.wait_ge(x1_ready, KD * g + k + 1)
                    last = pe.matmul(dst, wv_sb[:, k, m * P:(m + 1) * P], x1_t[:, k, :],
                                     start=(k == 0), stop=(k == KD - 1))
                last.then_inc(h0_done, 1)

            def transpose_pair(i):
                pe.wait_ge(tern_ready, i + 1)
                wait(pe, wt_ready, i)
                for b in range(2 * TT):
                    last = pe.transpose(ps_tr[:, b * P:(b + 1) * P], w_tern[:, i % RING, b * P:(b + 1) * P], ident_b[:])
                last.then_inc(tr_done, 1)

            def hidden(g, j):
                wait(pe, relued, HJ * g + j - RING + 1)
                if isinstance(g, int) and g == 0 and j % 2 == 0:
                    pe.wait_ge(wt_ready, [at for _, at in PAIRS].index(j) + 1)
                for k in range(KD):
                    if j == 0:
                        pe.wait_ge(h0_split, KD * g + k + 1)
                    for part in (h0_hi, h0_lo):
                        last = pe.matmul(ps_acc[:, j % RING, :], w_t[:, j, k * P:(k + 1) * P],
                                         part[:, k, bass.ds(g % RING * BANK, BANK)],
                                         start=(k == 0 and part is h0_hi), stop=(k == KD - 1 and part is h0_lo))
                last.then_inc(hid_done, 1)

            def project(g, j):
                c, i = j // TT, j % TT
                if isinstance(g, int) and g == 0 and i == 0:
                    pe.wait_ge(wt_ready, [at for _, at in PAIRS].index(HJ + KD * c + 2) + 1)
                pe.wait_ge(split, HJ * g + j + 1)
                w = w_t[:, HJ + KD * c:HJ + KD * (c + 1), i * P:(i + 1) * P]
                for t in range(TT):
                    if j == 0:
                        wait(pe, [even_copied, odd_copied][t % 2], (g - 1) * (TT // 2) + t // 2 + 1)
                    for part in (y_hi, y_lo):
                        last = pe.matmul(ps_out[:, t, :], part[:, j % RING, t * P:(t + 1) * P], w,
                                         start=(j == 0 and part is y_hi), stop=(j == HJ - 1 and part is y_lo))
                    if j == HJ - 1:
                        last.then_inc(tile_summed, 1)
                    if isinstance(g, int) and g == GROUPS - 1 and (j, t) == (HJ - 2, TT // 2):
                        sum_squares(g)
                if j < HJ - 1:
                    last.then_inc(projected, 1)

            def sum_squares(g):
                pe.wait_ge(sq_added, HJ * (g + 1))
                for t in range(TT):
                    last = pe.matmul(ps_sq[:, t:t + 1], sq_acc[:, t * P:(t + 1) * P], ones[:], start=True, stop=True)
                last.then_inc(sq_summed, 1)

            def group(g, pairs, more):
                x_at, h0_at = beside(g)
                for j in range(HJ):
                    if j + 1 < HJ and (more or j != HJ - 2):
                        hidden(g, j + 1)
                    if j == HJ - 3 and not more:
                        hidden(g, HJ - 1)
                    if j + 1 == HJ and more:
                        hidden(g + 1, 0)
                    if EARLY - 1 + j in pairs and EARLY - 1 + j in ON_PE:
                        transpose_pair(EARLY - 1 + j)
                    if j == 0 and not (isinstance(g, int) and g == 0):
                        pe.wait_ge(h0_relued, KD * (g + 1))
                        sum_squares(g - 1)
                    if more and j in x_at:
                        k = x_at[j]
                        if k == 0:
                            wait(pe, mean_ready, g)
                        else:
                            pe.wait_ge(x1_ready, KD * (g + 1) + k)
                        transpose_x(g + 1, k)
                    if more and j in h0_at:
                        m = h0_at[j]
                        if m == 0:
                            pe.wait_ge(x1_ready, KD * (g + 2))
                        else:
                            pe.wait_ge(h0_relued, KD * (g + 1) + m)
                        make_h0(g + 1, m, ps_x[:])
                    project(g, j)

            pe.wait_ge(consts_ready, 1)
            pe.wait_ge(cond_loaded, 16)
            for k in range(KQ):
                last = pe.transpose(ps_acc[:, 0, k * BATCHES:(k + 1) * BATCHES], cond_sb[:, k * P:(k + 1) * P],
                                    ident_f[0:BATCHES, 0:BATCHES])
            last.then_inc(condt_done, 1)
            for i in range(WARM_UP):
                pe.matmul(ps_x[:, 0:P], ident_b[:], ident_b[:], start=True, stop=True)
            for t in range(TT):
                if t == TT - 1:
                    pe.wait_ge(condt_ready, 1)
                    pe.wait_ge(wq_loaded, 16)
                    for m in range(KD):
                        for k in range(KQ):
                            last = pe.matmul(ps_acc[:, 1, m * BATCHES:(m + 1) * BATCHES], wq_sb[:, k, m * P:(m + 1) * P],
                                             cond_t[:, k, :], start=(k == 0), stop=(k == KQ - 1))
                    last.then_inc(q_done, 1)
                pe.wait_ge(x0_loaded[t], 16)
                for k in range(KD):
                    last = sum_x_block(t, k, ps_out[:, k, :])
                    if t == TT - 1:
                        last.then_inc(xt_done, 1)
            for m in range(KD):
                wait(pe, h0_relued, m - RING + 1)
                make_h0(0, m, ps_acc[:, m % RING, :])
                if m > 1:
                    transpose_pair(m - 2)
            transpose_x(1, 0)
            transpose_pair(EARLY - 2)
            hidden(0, 0)
            group(0, range(EARLY - 1, len(PAIRS)), True)
            with pe.Fori(1, GROUPS - 1) as g:
                group(g, [], True)
            group(GROUPS - 1, [], False)

        @block.vector
        def _(dve):
            def scaled(a):
                return a.rearrange("p (s w) -> p s w", w=TERN_GROUP)

            def spread(a):
                return a.rearrange("p (s o) -> p s o", o=1).to_broadcast([P, SG, TERN_GROUP])

            def scale_pair(i):
                r = i % RING
                dve.wait_ge(abs_ready, i + 1)
                dve.tensor_reduce(abs_sum[:], scaled(w_abs[:, r, :]), AX.X, ALU.add).then_inc(sum_ready, 1)
                dve.wait_ge(sum_ready, i + 1)
                wait(dve, signed, i - RING + 1)
                dve.tensor_scalar(scale[:, r, :], abs_sum[:], 1.0 / TERN_GROUP, MIN_SCALE,
                                  ALU.mult, ALU.max).then_inc(scale_ready, 1)
                dve.wait_ge(scale_ready, i + 1)
                dve.scalar_tensor_tensor(out=scaled(w_mask[:, r, :]), in0=scaled(w_abs[:, r, :]), scalar=2.0,
                                         in1=spread(scale[:, r, :]), op0=ALU.mult, op1=ALU.is_gt).then_inc(masked, 1)

            def ternary_pair(i):
                dve.wait_ge(masked, i + 1)
                dve.wait_ge(signed, i + 1)
                if i >= RING:
                    dve.wait_ge(*turned_at(i - RING))
                dve.tensor_tensor(w_tern[:, i % RING, :], w_mask[:, i % RING, :], w_signed[:, i % RING, :], ALU.mult).then_inc(tern_ready, 1)

            def scale_x(g, k, src):
                dve.wait_ge(xt_done, KD * g + k + 1)
                x1 = x1_t[:, k, :].rearrange("p (b n) -> p b n", n=N)
                src = src.rearrange("p (b n) -> p b n", n=N)
                if sums_by_vector(g):
                    dve.tensor_reduce(batch_sum[:], src, AX.X, ALU.add).then_inc(summed, 1)
                    dve.wait_ge(summed, 2 * (KD * (g - 2) + k) + 1)
                    dve.scalar_tensor_tensor(out=x1, in0=src, scalar=float(N),
                                             in1=batch_sum[:].rearrange("p (b o) -> p b o", o=1).to_broadcast([P, GB, N]),
                                             op0=ALU.mult, op1=ALU.add).then_inc(summed, 1)
                    dve.wait_ge(summed, 2 * (KD * (g - 2) + k) + 2)
                    src = x1
                dve.tensor_tensor(x1, src,
                                  q_t[:, k, bass.ds(g * GB, GB)].rearrange("p (b o) -> p b o", o=1).to_broadcast([P, GB, N]),
                                  ALU.mult).then_inc(x1_ready, 1)

            def round_h0(g, m):
                cols = bass.ds(g % RING * BANK, BANK)
                dve.wait_ge(h0_relued, KD * g + m + 1)
                dve.tensor_copy(h0_hi[:, m, cols], h0_f[:, m % RING, :]).then_inc(h0_hi_done, 1)

            def split_y(g, j):
                u = HJ * g + j
                dve.wait_ge(y_ready, u + 1)
                if j == 1:
                    wait(dve, tile_summed, TT * g)
                else:
                    wait(dve, projected, (HJ - 1) * g + max(j - RING + 1, 0))
                dve.tensor_copy(y_hi[:, j % RING, :], y[:, j % RING, :]).then_inc(hi_done, 1)
                dve.wait_ge(hi_done, u + 1)
                dve.tensor_tensor(y_lo[:, j % RING, :], y[:, j % RING, :], y_hi[:, j % RING, :], ALU.subtract).then_inc(split, 1)

            def mean_square(g):
                dve.wait_ge(sq_summed, g + 1)
                dve.tensor_scalar(mean_sq[:], ps_sq, 1.0 / H, RMS_EPS, ALU.mult, ALU.add).then_inc(mean_ready, 1)

            def inverse_root(g):
                dve.wait_ge(root_ready, g + 1)
                dve.reciprocal(rstd0[:], root[:]).then_inc(newton, 1)
                dve.wait_ge(newton, 3 * g + 1)
                dve.tensor_tensor(rsq[:], rstd0[:], rstd0[:], ALU.mult).then_inc(newton, 1)
                dve.wait_ge(newton, 3 * g + 2)
                dve.scalar_tensor_tensor(out=half[:], in0=mean_sq[:], scalar=-0.5, in1=rsq[:], op0=ALU.mult,
                                         op1=ALU.mult).then_inc(newton, 1)
                dve.wait_ge(newton, 3 * g + 3)
                dve.scalar_tensor_tensor(out=rstd[:], in0=half[:], scalar=1.5, in1=rstd0[:], op0=ALU.add,
                                         op1=ALU.mult).then_inc(rstd_ready, 1)

            def copy_even(g):
                wait(dve, stored, 16 * TT * g)
                for t in range(0, TT, 2):
                    dve.wait_ge(tile_summed, TT * g + t + 1)
                    dve.tensor_copy(o_sb[:, t, :], ps_out[:, t, :]).then_inc(even_copied, 1)

            def finish(g, t, sums):
                dve.wait_ge(rstd_ready, g + 1)
                dve.wait_ge(res_loaded, 16 * (g + 1))
                dve.scalar_tensor_tensor(out=o_sb[:, t, :], in0=sums[:, t, :], scalar=rstd[:, t:t + 1],
                                         in1=x_res[:, t, :], op0=ALU.mult, op1=ALU.add).then_inc(finished, 1)

            def group(g, pairs, more):
                x_at, h0_at = beside(g)
                later = not (isinstance(g, int) and g == 0)
                for j in range(HJ):
                    if EARLY + 1 + j in pairs:
                        scale_pair(EARLY + 1 + j)
                    if more and j - 1 in h0_at:
                        round_h0(g + 1, h0_at[j - 1])
                    if more and j in x_at and not later:
                        scale_x(g + 1, x_at[j], ps_x[:])
                    if EARLY + j in pairs:
                        ternary_pair(EARLY + j)
                    if j == HJ - 2 and not more:
                        add_squares(dve, g, HJ - 1)
                    if j + 1 < HJ:
                        split_y(g, j + 1)
                    elif more:
                        split_y(g + 1, 0)
                    if later and j == 0:
                        mean_square(g - 1)
                    if later and j == 1:
                        inverse_root(g - 1)
                    if more and j in x_at and later:
                        scale_x(g + 1, x_at[j], ps_x[:])
                    if later and j in FINISH_AT:
                        t = FINISH_AT[j]
                        dve.wait_ge([even_copied, odd_copied][t % 2], (g - 1) * (TT // 2) + t // 2 + 1)
                        finish(g - 1, t, o_sb)
                if more:
                    copy_even(g)

            dve.wait_ge(condt_done, 1)
            dve.tensor_copy(cond_t[:], ps_acc[:, 0, 0:KQ * BATCHES].rearrange("p (k b) -> p k b", k=KQ)).then_inc(condt_ready, 1)
            for k in range(KD):
                dve.wait_ge(q_ready, k + 1)
                scale_x(0, k, ps_out[:, k, :])
            scale_pair(0)
            for m in range(KD):
                if m + 1 < EARLY:
                    scale_pair(m + 1)
                ternary_pair(m)
                round_h0(0, m)
            dve.wait_ge(h0_split, KD - 1)
            rest_of_h0(dve, 0, KD - 1)
            scale_pair(EARLY)
            scale_x(1, 0, ps_x[:])
            split_y(0, 0)
            group(0, range(EARLY, len(PAIRS)), True)
            with dve.Fori(1, GROUPS - 1) as g:
                group(g, [], True)
            group(GROUPS - 1, [], False)
            mean_square(GROUPS - 1)
            inverse_root(GROUPS - 1)
            dve.wait_ge(stored, 16 * TT * (GROUPS - 1))
            for t in range(TT):
                dve.wait_ge(tile_summed, TT * (GROUPS - 1) + t + 1)
                finish(GROUPS - 1, t, ps_out)

        @block.scalar
        def _(act):
            def read_pair(i):
                r = i % RING
                act.wait_ge(raw_loaded[i % RAW_RING], 16 * (i // RAW_RING + 1))
                wait(act, masked, i - RING + 1)
                act.activation(w_abs[:, r, :], raw[:, i % RAW_RING, :], ACT.Abs).then_inc(abs_ready, 1)
                wait(act, signed, i - RING + 1)
                act.activation(w_sign[:, r, :], raw[:, i % RAW_RING, :], ACT.Sign).then_inc(sign_ready, 1)

            def keep_pair(i):
                src = ps_tr[:] if i in ON_PE else w_turned[:].rearrange("p b w -> p (b w)")
                at = PAIRS[i][1]
                act.wait_ge(*turned_at(i))
                act.activation(w_t[:, at:at + 2, :].rearrange("p i w -> p (i w)"), src, ACT.Copy).then_inc(wt_ready, 1)

            def relu_h0(g, m, src):
                act.wait_ge(h0_done, KD * g + m + 1)
                wait(act, h0_split, KD * g + m - RING + 1)
                act.activation(h0_f[:, m % RING, :], src, ACT.Relu, bias=bv_t[:, m:m + 1]).then_inc(h0_relued, 1)

            def relu_hidden(g, j):
                act.wait_ge(hid_done, HJ * g + j + 1)
                act.activation(relu_y[:, j % RING, :], ps_acc[:, j % RING, :], ACT.Relu).then_inc(relued, 1)

            def square_relu(g, j):
                u = HJ * g + j
                act.wait_ge(relued, u + 1)
                wait(act, split, u - RING + 1)
                act.activation(y[:, j % RING, :], relu_y[:, j % RING, :], ACT.Square).then_inc(y_ready, 1)

            def square_y(g, j):
                u = HJ * g + j
                act.wait_ge(y_ready, u + 1)
                wait(act, sq_added, u - SQ_RING + 1)
                act.activation(y_sq[:, j % SQ_RING, :], y[:, j % RING, :], ACT.Square).then_inc(sq_ready, 1)

            def take_root(g):
                act.wait_ge(mean_ready, g + 1)
                act.activation(root[:], mean_sq[:], ACT.Sqrt).then_inc(root_ready, 1)

            def copy_odd(g):
                wait(act, stored, 16 * TT * g)
                for t in range(1, TT, 2):
                    act.wait_ge(tile_summed, TT * g + t + 1)
                    act.activation(o_sb[:, t, :], ps_out[:, t, :], ACT.Copy).then_inc(odd_copied, 1)

            def group(g, pairs, more):
                x_at, h0_at = beside(g)
                for j in range(HJ):
                    tile = (g, j + 1) if j + 1 < HJ else (g + 1, 0)
                    last = j + 1 == HJ and not more
                    if not last:
                        relu_hidden(*tile)
                    if EARLY - 1 + j in pairs and EARLY - 1 + j in ON_PE:
                        keep_pair(EARLY - 1 + j)
                    if not last:
                        square_relu(*tile)
                    if j == 1 and not (isinstance(g, int) and g == 0):
                        take_root(g - 1)
                    if not last:
                        square_y(*tile)
                    if EARLY - 1 + j in pairs and EARLY - 1 + j not in ON_PE:
                        keep_pair(EARLY - 1 + j)
                    if EARLY + 2 + j in pairs:
                        read_pair(EARLY + 2 + j)
                    if more and j in h0_at:
                        relu_h0(g + 1, h0_at[j], ps_x[:])
                if more:
                    copy_odd(g)

            act.dma_start(bq_t[:], b_q.rearrange("(m p) -> p m", p=P), allow_slow_non_contiguous=True).then_inc(bias_loaded, 16)
            act.dma_start(bv_t[:], b_v.rearrange("(m p) -> p m", p=P), allow_slow_non_contiguous=True).then_inc(bias_loaded, 16)
            act.wait_ge(consts_ready, 1)
            act.activation(root[:, 0:1], ones[:], ACT.Sqrt)
            act.wait_ge(bias_loaded, 32)
            act.wait_ge(q_done, 1)
            for m in range(KD):
                act.activation(q_t[:, m, :], ps_acc[:, 1, m * BATCHES:(m + 1) * BATCHES], ACT.Relu,
                               bias=bq_t[:, m:m + 1]).then_inc(q_ready, 1)
            read_pair(0)
            for m in range(KD):
                read_pair(m + 1)
                relu_h0(0, m, ps_acc[:, m % RING, :])
                if m > 1:
                    keep_pair(m - 2)
            read_pair(EARLY + 1)
            keep_pair(EARLY - 2)
            relu_hidden(0, 0)
            square_relu(0, 0)
            square_y(0, 0)
            group(0, range(EARLY - 1, len(PAIRS)), True)
            with act.Fori(1, GROUPS - 1) as g:
                group(g, [], True)
            group(GROUPS - 1, [], False)
            take_root(GROUPS - 1)

        @block.gpsimd
        def _(pool):
            def sign_pair(i):
                pool.wait_ge(sign_ready, i + 1)
                pool.wait_ge(scale_ready, i + 1)
                wait(pool, tern_ready, i - RING + 1)
                pool.tensor_tensor(w_signed[:, i % RING, :].rearrange("p (s w) -> p s w", w=TERN_GROUP),
                                   w_sign[:, i % RING, :].rearrange("p (s w) -> p s w", w=TERN_GROUP),
                                   scale[:, i % RING, :].rearrange("p (s o) -> p s o", o=1).to_broadcast([P, SG, TERN_GROUP]),
                                   ALU.mult).then_inc(signed, 1)

            def group(g, pairs, more):
                x_at, h0_at = beside(g)
                for j in range(HJ):
                    if EARLY + 1 + j in pairs:
                        sign_pair(EARLY + 1 + j)
                    if j > 0 and (more or j < HJ - 1):
                        add_squares(pool, g, j)
                    if more and j - 1 in h0_at:
                        rest_of_h0(pool, g + 1, h0_at[j - 1])

            pool.memset(sum_mat[:], 0.0).then_inc(cleared, 1)
            pool.memset(ident_b[:], 0.0).then_inc(cleared, 1)
            pool.memset(ident_f[:], 0.0).then_inc(cleared, 1)
            pool.memset(ones[:], 1.0).then_inc(cleared, 1)
            pool.wait_ge(cleared, 4)
            for b in range(P // N):
                pool.memset(sum_mat[b * N:(b + 1) * N, b * N:(b + 1) * N], 1.0).then_inc(cleared, 1)
            pool.wait_ge(cleared, 4 + P // N)
            pool.affine_select(out=sum_mat[:], in_=sum_mat[:], compare_op=ALU.not_equal, fill=float(N + 1), base=0,
                               pattern=[[-1, P]], channel_multiplier=1).then_inc(cleared, 1)
            pool.affine_select(out=ident_b[:], in_=ident_b[:], compare_op=ALU.not_equal, fill=1.0, base=0,
                               pattern=[[-1, P]], channel_multiplier=1).then_inc(cleared, 1)
            pool.affine_select(out=ident_f[:], in_=ident_f[:], compare_op=ALU.not_equal, fill=1.0, base=0,
                               pattern=[[-1, P]], channel_multiplier=1).then_inc(cleared, 1)
            pool.wait_ge(cleared, 7 + P // N)
            pool.nop().then_inc(consts_ready, 1)

            sign_pair(0)
            for m in range(KD - 1):
                sign_pair(m + 1)
                rest_of_h0(pool, 0, m)
            sign_pair(EARLY)
            group(0, range(EARLY, len(PAIRS)), True)
            with pool.Fori(1, GROUPS - 1) as g:
                group(g, [], True)
            group(GROUPS - 1, [], False)


_INS = ['x', 'cond_1024', 'L0_cond_W3', 'L0_cond_b3', 'L0_cond_W2', 'L0_cond_b2', 'L0_ffn_W_fc', 'L0_ffn_W_proj']
_OUTS = [((32, 64, 512), 'float32')]


def kernel(**inputs):
    import numpy as _np
    import concourse.bacc as _bacc
    from concourse import mybir as _mybir
    from concourse.bass_utils import run_bass_kernel_spmd as _run

    nc = _bacc.Bacc("TRN2", target_bir_lowering=False, num_devices=1)
    arrays, args = {}, []
    for name in _INS:
        a = _np.ascontiguousarray(inputs[name])
        arrays[f"in_{name}_dram"] = a
        args.append(nc.dram_tensor(f"in_{name}_dram", a.shape, _mybir.dt.from_np(a.dtype), kind="ExternalInput").ap())
    for i, (shape, dtype) in enumerate(_OUTS):
        dt = _mybir.dt.from_np(_np.dtype(dtype))
        args.append(nc.dram_tensor(f"out_{i}_dram", shape, dt, kind="ExternalOutput").ap())
    adaln_ffn(nc, *args)
    r = _run(nc, [arrays], core_ids=[0])
    return r.results[0]["out_0_dram"]
```
